# Optimizing a Trainium2 kernel written in Bass

```python
import numpy as np
import jax
import jax.numpy as jnp

def _softmax(x, axis=-1):
    return jax.nn.softmax(x, axis=axis)

def _gelu(x):
    return jax.nn.gelu(x, approximate=True)

def _silu(x):
    return jax.nn.silu(x)

def _sigmoid(x):
    return jax.nn.sigmoid(x)

def _layernorm(x, axis=-1, eps=1e-05):
    m = jnp.mean(x, axis=axis, keepdims=True)
    v = jnp.var(x, axis=axis, keepdims=True)
    return (x - m) / jnp.sqrt(v + eps)

def _scatter_add(tgt, idx, src, axis=0):
    return tgt.at[idx].add(src)

def _segment_sum(src, seg, n):
    return jax.ops.segment_sum(src, seg, n)
kernel_name = 'mk_adj_resnorm_d1_adj_r2_49085e'

def setup_inputs(seed: int=0):
    np.random.seed(seed)
    _w = jnp.asarray

    def _rec_inputs():
        import jax
        import jax.numpy as jnp
        _gk = jax.random.key(seed)
        x = -0.0006008 + 1.001 * jax.random.normal(jax.random.fold_in(_gk, 1), (8192, 128), jnp.float32)
        _a = jax.random.bernoulli(jax.random.fold_in(_gk, 2), 0.000976562, (8192, 8192))
        _a = jnp.logical_or(_a, jnp.eye(8192, dtype=bool))
        _af = _a.astype(jnp.float32)
        _af = _af * jax.random.uniform(jax.random.fold_in(_gk, 3), (8192, 8192), jnp.float32, 0.05, 1)
        adj = _af
        return (x, adj)
    x, adj = _rec_inputs()

    def _L0_gnn_setup():
        import jax, jax.numpy as jnp
        import numpy as np
        N = 5000
        F = 128
        key = jax.random.key(seed)
        k1, k2 = jax.random.split(key)
        x = jax.random.normal(k1, (N, F), dtype=jnp.float32)
        A = jax.random.uniform(k2, (N, N), dtype=jnp.float32)
        W = jnp.ones((F,), dtype=jnp.float32)
        return {'input': x, 'A': A, 'W': W}
    _L0_gnn_all = _L0_gnn_setup()
    _L0_gnn_in = {k: v for k, v in _L0_gnn_all.items() if k in ('W',)}
    del _L0_gnn_all
    return {'x': x, 'adj': adj, 'L0_gnn_W': _L0_gnn_in['W']}

def reference(x, adj, L0_gnn_W):
    import jax
    import jax.numpy as jnp

    def _L0_gnn_ref(input, A, W):
        import jax, jax.numpy as jnp
        import numpy as np
        N = 5000
        F = 128
        hidden = input * W
        return A @ hidden
    x = _layernorm(x + _L0_gnn_ref(x, adj, L0_gnn_W), axis=-1)
    return x

_drawn_inputs = setup_inputs


def setup_inputs(seed=0):
    import zlib

    import numpy as np

    out = dict(_drawn_inputs(seed))
    spreads = {'L0_gnn_W': (1.0, 0.2)}
    factors = {}
    for name, (base, spread) in spreads.items():
        noise = np.random.default_rng([zlib.crc32(name.encode()), seed]).standard_normal(out[name].shape)
        drawn = base * np.exp(spread * noise) if base else spread * noise
        out[name] = jnp.asarray(drawn.astype(out[name].dtype))
    for name, factor in factors.items():
        out[name] = (out[name] * factor).astype(out[name].dtype)
    return out
```

```python
from contextlib import ExitStack

import concourse.bass as bass
from concourse import mybir

F32 = mybir.dt.float32
F32R = mybir.dt.float32r
ALU = mybir.AluOpType
ACT = mybir.ActivationFunctionType

P = 128
ROWS = 512
CHUNKS = 4
RING = 4
EPS = 1e-5

COPY_AFTER = 3
TURN_AFTER = 1
STATS_AFTER = 6
SQRT_AFTER = 8
NORM_AFTER = 10
STORE_AFTER = 15


def resnorm_program(nc, x, adj, w, ident, out):
    _, NC, F = x.shape
    TILES = adj.shape[0]
    TPG = NC // CHUNKS
    GROUPS = TILES // TPG
    BLOCKS = ROWS // P
    LAPS = TPG // RING
    assert F == P and TPG % RING == 0 and GROUPS * ROWS == NC * P

    with ExitStack() as ctx:
        def sb(name, shape, dt=F32):
            return ctx.enter_context(nc.sbuf_tensor(name, shape, dt))

        def sem(name):
            return ctx.enter_context(nc.semaphore(name))

        x_sb = sb("x_sb", [P, NC, F])
        h_hi = sb("h_hi", [P, NC, F], F32R)
        h_lo = sb("h_lo", [P, NC, F], F32R)
        h_full = sb("h_full", [P, 2, CHUNKS, F])
        w_sb = sb("w_sb", [P, F])
        ident_sb = sb("ident_sb", [P, P])
        raw = sb("raw", [P, RING, CHUNKS, ROWS])
        a_hi = sb("a_hi", [P, RING, CHUNKS, ROWS], F32R)
        a_lo = sb("a_lo", [P, RING, CHUNKS, ROWS], F32R)
        yT = sb("yT", [P, ROWS])
        z = sb("z", [P, BLOCKS, F])
        stats = sb("stats", [P, BLOCKS, 6])
        mean = sb("mean", [P, BLOCKS])
        gap = sb("gap", [P, BLOCKS])
        within = sb("within", [P, BLOCKS])
        var = sb("var", [P, BLOCKS])
        root = sb("root", [P, BLOCKS])
        rstd0 = sb("rstd0", [P, BLOCKS])
        newton = sb("newton", [P, BLOCKS])
        rstd = sb("rstd", [P, BLOCKS])
        o_sb = sb("o_sb", [P, BLOCKS, F])

        sums = ctx.enter_context(nc.psum_tensor("sums", [P, 2, ROWS], F32))
        turned = ctx.enter_context(nc.psum_tensor("turned", [P, BLOCKS, F], F32))

        consts_loaded = sem("consts_loaded")
        x_loaded = [sem(f"x_loaded{i}") for i in range(2)]
        tile_loaded = [sem(f"tile_loaded{s}") for s in range(RING)]
        h_made = sem("h_made")
        h_hi_made = sem("h_hi_made")
        h_lo_made = sem("h_lo_made")
        hi_made = sem("hi_made")
        lo_made = sem("lo_made")
        tile_used = sem("tile_used")
        sums_copied = sem("sums_copied")
        sums_turned = sem("sums_turned")
        z_made = sem("z_made")
        vec_step = sem("vec_step")
        var_made = sem("var_made")
        root_made = sem("root_made")
        rows_made = sem("rows_made")
        rows_stored = sem("rows_stored")

        STATS_STEPS = 1 + BLOCKS + 6
        VEC_STEPS = STATS_STEPS + 5

        block = ctx.enter_context(nc.Block())

        @block.sync
        def _(sp):
            def load(g, k):
                slot = k % RING
                sp.dma_start(raw[:, slot], adj[g * TPG + k]).then_inc(tile_loaded[slot], 16)

            def store(g):
                sp.wait_ge(rows_made, (g + 1) * BLOCKS)
                sp.dma_start(out[g], o_sb[:, :, :]).then_inc(rows_stored, 16)

            sp.dma_start(w_sb[:, :], w[:, :].to_broadcast([P, F])).then_inc(consts_loaded, 16)
            sp.dma_start(ident_sb[:, :], ident).then_inc(consts_loaded, 16)
            for k in range(TPG):
                cs = slice(k * CHUNKS, (k + 1) * CHUNKS)
                if k >= 2:
                    sp.wait_ge(h_made, k - 1)
                sp.dma_start(x_sb[:, cs], x[:, cs]).then_inc(x_loaded[k % 2], 16)
                if k >= RING:
                    sp.wait_ge(lo_made, k - RING + 1)
                load(0, k)
            with sp.Fori(1, GROUPS) as g:
                for k in range(TPG):
                    sp.wait_ge(lo_made, g * TPG + (k - RING + 1))
                    load(g, k)
                store(g - 1)
            store(GROUPS - 1)
            sp.wait_ge(rows_stored, 16 * GROUPS)

        @block.scalar
        def _(act):
            def split_tile(g, k):
                slot = k % RING
                act.wait_ge(tile_loaded[slot], (g * LAPS + (k // RING + 1)) * 16)
                if not (isinstance(g, int) and g == 0 and k < RING):
                    act.wait_ge(tile_used, g * TPG + (k - RING + 1))
                act.activation(a_hi[:, slot], raw[:, slot], ACT.Copy).then_inc(hi_made, 1)

            def copy_sums(g, bank):
                act.wait_ge(tile_used, (g + 1) * TPG)
                act.activation(yT[:, :], sums[:, bank], ACT.Copy).then_inc(sums_copied, 1)

            def take_root(g):
                act.wait_ge(var_made, g + 1)
                act.activation(root[:, :], var[:, :], ACT.Sqrt).then_inc(root_made, 1)

            for k in range(TPG):
                cs = slice(k * CHUNKS, (k + 1) * CHUNKS)
                act.wait_ge(h_made, k + 1)
                act.activation(h_hi[:, cs], h_full[:, k % 2], ACT.Copy).then_inc(h_hi_made, 1)
                split_tile(0, k)
            with act.Fori(1, GROUPS) as g:
                for k in range(TPG):
                    split_tile(g, k)
                    if k == COPY_AFTER:
                        copy_sums(g - 1, (g - 1) % 2)
                    if k == SQRT_AFTER:
                        take_root(g - 1)
            copy_sums(GROUPS - 1, (GROUPS - 1) % 2)
            take_root(GROUPS - 1)

        @block.gpsimd
        def _(pool):
            for k in range(TPG):
                cs = slice(k * CHUNKS, (k + 1) * CHUNKS)
                pool.wait_ge(h_hi_made, k + 1)
                pool.tensor_tensor(h_lo[:, cs], h_full[:, k % 2], h_hi[:, cs].bitcast(F32),
                                   ALU.subtract).then_inc(h_lo_made, 1)

        @block.vector
        def _(vec):
            def split_tile(g, k):
                slot = k % RING
                vec.wait_ge(hi_made, g * TPG + (k + 1))
                vec.tensor_tensor(a_lo[:, slot], raw[:, slot], a_hi[:, slot].bitcast(F32),
                                  ALU.subtract).then_inc(lo_made, 1)

            def residual_and_stats(g):
                done = g * VEC_STEPS
                vec.wait_ge(sums_turned, g + 1)
                vec.tensor_tensor(z[:, :, :], turned[:, :, :], x_sb[:, bass.ds(g * BLOCKS, BLOCKS)],
                                  ALU.add).then_inc(vec_step, 1)
                vec.wait_ge(vec_step, done + 1)
                for b in range(BLOCKS):
                    vec.bn_stats(stats[:, b], z[:, b]).then_inc(vec_step, 1)
                vec.wait_ge(vec_step, done + (1 + BLOCKS))
                vec.tensor_tensor(mean[:, :], stats[:, :, 1], stats[:, :, 4], ALU.add).then_inc(vec_step, 1)
                vec.tensor_tensor(gap[:, :], stats[:, :, 1], stats[:, :, 4], ALU.subtract).then_inc(vec_step, 1)
                vec.tensor_tensor(within[:, :], stats[:, :, 2], stats[:, :, 5], ALU.add).then_inc(vec_step, 1)
                vec.wait_ge(vec_step, done + (4 + BLOCKS))
                vec.tensor_scalar(mean[:, :], mean[:, :], 0.5, None, ALU.mult).then_inc(vec_step, 1)
                vec.tensor_tensor(gap[:, :], gap[:, :], gap[:, :], ALU.mult).then_inc(vec_step, 1)
                vec.tensor_scalar(within[:, :], within[:, :], 1.0 / F, EPS, ALU.mult, ALU.add)\
                   .then_inc(vec_step, 1)
                vec.wait_ge(vec_step, done + (7 + BLOCKS))
                vec.scalar_tensor_tensor(out=var[:, :], in0=gap[:, :], scalar=0.25, in1=within[:, :],
                                         op0=ALU.mult, op1=ALU.add).then_inc(var_made, 1)

            def normalise(g):
                done = g * VEC_STEPS + STATS_STEPS
                vec.wait_ge(root_made, g + 1)
                vec.reciprocal(rstd0[:, :], root[:, :]).then_inc(vec_step, 1)
                vec.wait_ge(vec_step, done + 1)
                vec.tensor_tensor(newton[:, :], rstd0[:, :], rstd0[:, :], ALU.mult).then_inc(vec_step, 1)
                vec.wait_ge(vec_step, done + 2)
                vec.tensor_tensor(newton[:, :], newton[:, :], var[:, :], ALU.mult).then_inc(vec_step, 1)
                vec.wait_ge(vec_step, done + 3)
                vec.tensor_scalar(newton[:, :], newton[:, :], -0.5, 1.5, ALU.mult, ALU.add)\
                   .then_inc(vec_step, 1)
                vec.wait_ge(vec_step, done + 4)
                vec.tensor_tensor(rstd[:, :], rstd0[:, :], newton[:, :], ALU.mult).then_inc(vec_step, 1)
                vec.wait_ge(vec_step, done + 5)
                if not (isinstance(g, int) and g == 0):
                    vec.wait_ge(rows_stored, g * 16)
                for b in range(BLOCKS):
                    vec.tensor_scalar(o_sb[:, b], z[:, b], mean[:, b:b + 1], rstd[:, b:b + 1],
                                      ALU.subtract, ALU.mult).then_inc(rows_made, 1)

            def hidden(k):
                cs = slice(k * CHUNKS, (k + 1) * CHUNKS)
                vec.wait_ge(x_loaded[k % 2], 16 * (k // 2 + 1))
                if k >= 2:
                    vec.wait_ge(h_lo_made, k - 1)
                vec.tensor_tensor(h_full[:, k % 2], x_sb[:, cs],
                                  w_sb[:, :].unsqueeze(1).to_broadcast([P, CHUNKS, F]),
                                  ALU.mult).then_inc(h_made, 1)

            vec.wait_ge(consts_loaded, 32)
            hidden(0)
            for k in range(TPG):
                if k + 1 < TPG:
                    hidden(k + 1)
                split_tile(0, k)
            with vec.Fori(1, GROUPS) as g:
                for k in range(TPG):
                    split_tile(g, k)
                    if k == STATS_AFTER:
                        residual_and_stats(g - 1)
                    if k == NORM_AFTER:
                        normalise(g - 1)
            residual_and_stats(GROUPS - 1)
            normalise(GROUPS - 1)

        @block.tensor
        def _(pe):
            def products(g, k, bank):
                slot = k % RING
                pe.wait_ge(hi_made, g * TPG + (k + 1))
                for c in range(CHUNKS):
                    pe.matmul(sums[:, bank], h_hi[:, k * CHUNKS + c], a_hi[:, slot, c],
                              start=(k == 0 and c == 0), stop=False)
                    pe.matmul(sums[:, bank], h_lo[:, k * CHUNKS + c], a_hi[:, slot, c],
                              start=False, stop=False)
                pe.wait_ge(lo_made, g * TPG + (k + 1))
                for c in range(CHUNKS):
                    mm = pe.matmul(sums[:, bank], h_hi[:, k * CHUNKS + c], a_lo[:, slot, c],
                                   start=False, stop=(k == TPG - 1 and c == CHUNKS - 1))
                mm.then_inc(tile_used, 1)

            def turn(g):
                pe.wait_ge(sums_copied, g + 1)
                for b in range(BLOCKS):
                    t = pe.transpose(turned[:, b], yT[:, b * P:(b + 1) * P], ident_sb[:, :])
                t.then_inc(sums_turned, 1)

            for k in range(TPG):
                pe.wait_ge(h_lo_made, k + 1)
                products(0, k, 0)
            pe.wait_ge(consts_loaded, 32)
            with pe.Fori(1, GROUPS) as g:
                for k in range(TPG):
                    products(g, k, g % 2)
                    if k == TURN_AFTER:
                        turn(g - 1)
            turn(GROUPS - 1)


def kernel(x, adj, L0_gnn_W):
    import numpy as np
    import concourse.bacc as bacc
    from concourse.bass_utils import run_bass_kernel_spmd

    n, f = x.shape
    groups, chunks = n // ROWS, n // P
    arrays = {
        "x_l": np.ascontiguousarray(np.asarray(x).reshape(chunks, P, f).transpose(1, 0, 2)),
        "adj_l": np.ascontiguousarray(
            np.asarray(adj).reshape(groups, ROWS, chunks // CHUNKS, CHUNKS, P).transpose(0, 2, 4, 3, 1)
        ).reshape(groups * chunks // CHUNKS, P, CHUNKS, ROWS),
        "w_l": np.asarray(L0_gnn_W).reshape(1, f),
        "ident_l": np.eye(P, dtype=np.float32),
    }
    nc = bacc.Bacc("TRN2", target_bir_lowering=False, num_devices=1)
    aps = [nc.dram_tensor(name, a.shape, F32, kind="ExternalInput").ap() for name, a in arrays.items()]
    out = nc.dram_tensor("out_l", [groups, P, ROWS // P, f], F32, kind="ExternalOutput").ap()
    resnorm_program(nc, *aps, out)
    r = run_bass_kernel_spmd(nc, [arrays], core_ids=[0])
    return r.results[0]["out_l"].transpose(0, 2, 1, 3).reshape(n, f)
```

```python
from contextlib import ExitStack

import concourse.bass as bass
from concourse import mybir

F32 = mybir.dt.float32
F32R = mybir.dt.float32r
ALU = mybir.AluOpType
ACT = mybir.ActivationFunctionType

P = 128
ROWS = 512
CHUNKS = 4
RING = 4
EPS = 1e-5

COPY_AFTER = 2
TURN_AFTER = 2
STATS_AFTER = 4
ROOT_AFTER = 6
NORM_AFTER = 7
STORE_AFTER = 15


def resnorm_program(nc, x, adj, w, ident, out):
    _, NC, F = x.shape
    TILES = adj.shape[0]
    TPG = NC // CHUNKS
    GROUPS = TILES // TPG
    BLOCKS = ROWS // P
    LAPS = TPG // RING
    assert F == P and TPG % RING == 0 and GROUPS * ROWS == NC * P

    def steps(g, k):
        if isinstance(g, int) and g == GROUPS - 1:
            return [(slice(c, c + 1), g * TPG + k * CHUNKS + c + 1) for c in range(CHUNKS)]
        return [(slice(0, CHUNKS), g * TPG + (k + 1))]

    def made_after(g, k):
        return steps(g, k)[-1][1] if k >= 0 else g * TPG + (k + 1)

    def is_fine(chunks):
        return chunks.stop - chunks.start < CHUNKS

    with ExitStack() as ctx:
        def sb(name, shape, dt=F32):
            return ctx.enter_context(nc.sbuf_tensor(name, shape, dt))

        def sem(name):
            return ctx.enter_context(nc.semaphore(name))

        x_sb = sb("x_sb", [P, NC, F])
        h_hi = sb("h_hi", [P, NC, F], F32R)
        h_lo = sb("h_lo", [P, NC, F], F32R)
        h_full = sb("h_full", [P, 2, CHUNKS, F])
        w_sb = sb("w_sb", [P, F])
        ident_sb = sb("ident_sb", [P, P])
        raw = sb("raw", [P, RING, CHUNKS, ROWS])
        a_hi = sb("a_hi", [P, RING, CHUNKS, ROWS], F32R)
        a_lo = sb("a_lo", [P, RING, CHUNKS, ROWS], F32R)
        yT = sb("yT", [P, ROWS])
        z = sb("z", [P, BLOCKS, F])
        stats = sb("stats", [P, BLOCKS, 6])
        mean = sb("mean", [P, BLOCKS])
        gap = sb("gap", [P, BLOCKS])
        within = sb("within", [P, BLOCKS])
        var = sb("var", [P, BLOCKS])
        root = sb("root", [P, BLOCKS])
        rstd0 = sb("rstd0", [P, BLOCKS])
        newton = sb("newton", [P, BLOCKS])
        rstd = sb("rstd", [P, BLOCKS])
        o_sb = sb("o_sb", [P, BLOCKS, F])

        sums = ctx.enter_context(nc.psum_tensor("sums", [P, 2, ROWS], F32))
        turned = ctx.enter_context(nc.psum_tensor("turned", [P, BLOCKS, F], F32))

        consts_then_rows = sem("consts_then_rows")
        x_loaded = [sem(f"x_loaded{i}") for i in range(2)]
        tile_loaded = [sem(f"tile_loaded{s}") for s in range(RING)]
        chunk_loaded = [[sem(f"chunk_loaded{s}_{c}") for c in range(CHUNKS)] for s in range(RING)]
        h_made = sem("h_made")
        h_hi_made = sem("h_hi_made")
        h_lo_made = sem("h_lo_made")
        hi_made = sem("hi_made")
        lo_made = sem("lo_made")
        tile_used = sem("tile_used")
        sums_copied = sem("sums_copied")
        sums_turned = sem("sums_turned")
        vec_step = sem("vec_step")
        var_made = sem("var_made")
        root_made = sem("root_made")
        rows_made = sem("rows_made")

        CONSTS = 2 * 16
        STATS_STEPS = 1 + BLOCKS + 6
        VEC_STEPS = STATS_STEPS + 4

        block = ctx.enter_context(nc.Block())

        @block.sync
        def _(sp):
            def load(g, k):
                slot = k % RING
                for chunks, _ in steps(g, k):
                    signal = tile_loaded[slot]
                    if is_fine(chunks):
                        signal = chunk_loaded[slot][chunks.start]
                    sp.dma_start(raw[:, slot, chunks], adj[g * TPG + k, :, chunks]).then_inc(signal, 16)

            def store(g, b0=0, b1=BLOCKS):
                sp.wait_ge(rows_made, g * BLOCKS + b1)
                sp.dma_start(out[g, :, b0:b1], o_sb[:, b0:b1]).then_inc(consts_then_rows, 16)

            for k in range(TPG):
                cs = slice(k * CHUNKS, (k + 1) * CHUNKS)
                if k >= 2:
                    sp.wait_ge(h_made, k - 1)
                sp.dma_start(x_sb[:, cs], x[:, cs]).then_inc(x_loaded[k % 2], 16)
                if k == 0:
                    sp.dma_start(w_sb[:, :], w[:, :].to_broadcast([P, F])).then_inc(consts_then_rows, 16)
                    sp.dma_start(ident_sb[:, :], ident).then_inc(consts_then_rows, 16)
                if k >= RING:
                    sp.wait_ge(lo_made, k - RING + 1)
                load(0, k)

            def later_group(g):
                for k in range(TPG):
                    sp.wait_ge(lo_made, made_after(g, k - RING))
                    load(g, k)
                    if k == STORE_AFTER:
                        store(g - 1)

            with sp.Fori(1, GROUPS - 1) as g:
                later_group(g)
            later_group(GROUPS - 1)
            store(GROUPS - 1, 0, BLOCKS // 2)
            store(GROUPS - 1, BLOCKS // 2, BLOCKS)
            sp.wait_ge(consts_then_rows, CONSTS + 16 * (GROUPS + 1))

        @block.scalar
        def _(act):
            def split_tile(g, k):
                slot = k % RING
                if not (isinstance(g, int) and g == 0 and k < RING):
                    act.wait_ge(tile_used, g * TPG + (k - RING + 1))
                for chunks, _ in steps(g, k):
                    if is_fine(chunks):
                        act.wait_ge(chunk_loaded[slot][chunks.start], 16 * (k // RING + 1))
                    else:
                        act.wait_ge(tile_loaded[slot], (g * LAPS + (k // RING + 1)) * 16)
                    act.activation(a_hi[:, slot, chunks], raw[:, slot, chunks], ACT.Copy).then_inc(hi_made, 1)

            def copy_sums(g, bank):
                act.wait_ge(tile_used, (g + 1) * TPG)
                act.activation(yT[:, :], sums[:, bank], ACT.Copy).then_inc(sums_copied, 1)

            def take_root(g):
                act.wait_ge(var_made, g + 1)
                act.activation(root[:, :], var[:, :], ACT.Sqrt).then_inc(root_made, 1)

            act.activation(root[0:1, 0:1], nc.const_aps.tensor(1.0, (1, 1), F32), ACT.Sqrt)
            for k in range(TPG):
                cs = slice(k * CHUNKS, (k + 1) * CHUNKS)
                act.wait_ge(h_made, k + 1)
                act.activation(h_hi[:, cs], h_full[:, k % 2], ACT.Copy).then_inc(h_hi_made, 1)
                split_tile(0, k)

            def later_group(g):
                for k in range(TPG):
                    split_tile(g, k)
                    if k == COPY_AFTER:
                        copy_sums(g - 1, (g - 1) % 2)
                    if k == ROOT_AFTER:
                        take_root(g - 1)

            with act.Fori(1, GROUPS - 1) as g:
                later_group(g)
            later_group(GROUPS - 1)
            copy_sums(GROUPS - 1, (GROUPS - 1) % 2)
            take_root(GROUPS - 1)

        @block.gpsimd
        def _(pool):
            for k in range(TPG):
                cs = slice(k * CHUNKS, (k + 1) * CHUNKS)
                pool.wait_ge(h_hi_made, k + 1)
                pool.tensor_tensor(h_lo[:, cs], h_full[:, k % 2], h_hi[:, cs].bitcast(F32),
                                   ALU.subtract).then_inc(h_lo_made, 1)

        @block.vector
        def _(vec):
            def split_tile(g, k):
                slot = k % RING
                for chunks, made in steps(g, k):
                    vec.wait_ge(hi_made, made)
                    vec.tensor_tensor(a_lo[:, slot, chunks], raw[:, slot, chunks],
                                      a_hi[:, slot, chunks].bitcast(F32), ALU.subtract).then_inc(lo_made, 1)

            def residual(g):
                done = g * VEC_STEPS
                vec.wait_ge(sums_turned, g + 1)
                vec.tensor_tensor(z[:, :, :], turned[:, :, :], x_sb[:, bass.ds(g * BLOCKS, BLOCKS)],
                                  ALU.add).then_inc(vec_step, 1)
                vec.wait_ge(vec_step, done + 1)
                for b in range(BLOCKS // 2):
                    vec.bn_stats(stats[:, b], z[:, b]).then_inc(vec_step, 1)

            def variance(g):
                done = g * VEC_STEPS
                for b in range(BLOCKS // 2, BLOCKS):
                    vec.bn_stats(stats[:, b], z[:, b]).then_inc(vec_step, 1)
                vec.wait_ge(vec_step, done + (1 + BLOCKS))
                vec.tensor_tensor(mean[:, :], stats[:, :, 1], stats[:, :, 4], ALU.add).then_inc(vec_step, 1)
                vec.tensor_tensor(gap[:, :], stats[:, :, 1], stats[:, :, 4], ALU.subtract).then_inc(vec_step, 1)
                vec.tensor_tensor(within[:, :], stats[:, :, 2], stats[:, :, 5], ALU.add).then_inc(vec_step, 1)
                vec.wait_ge(vec_step, done + (4 + BLOCKS))
                vec.tensor_scalar(mean[:, :], mean[:, :], 0.5, None, ALU.mult).then_inc(vec_step, 1)
                vec.tensor_tensor(gap[:, :], gap[:, :], gap[:, :], ALU.mult).then_inc(vec_step, 1)
                vec.tensor_scalar(within[:, :], within[:, :], 1.0 / F, EPS, ALU.mult, ALU.add)\
                   .then_inc(vec_step, 1)
                vec.wait_ge(vec_step, done + (7 + BLOCKS))
                vec.scalar_tensor_tensor(out=var[:, :], in0=gap[:, :], scalar=0.25, in1=within[:, :],
                                         op0=ALU.mult, op1=ALU.add).then_inc(var_made, 1)

            def factor(g):
                done = g * VEC_STEPS + STATS_STEPS
                vec.wait_ge(root_made, g + 1)
                vec.reciprocal(rstd0[:, :], root[:, :]).then_inc(vec_step, 1)
                vec.wait_ge(vec_step, done + 1)
                vec.scalar_tensor_tensor(out=newton[:, :], in0=rstd0[:, :], scalar=-0.5, in1=rstd0[:, :],
                                         op0=ALU.mult, op1=ALU.mult).then_inc(vec_step, 1)
                vec.wait_ge(vec_step, done + 2)
                vec.tensor_tensor(newton[:, :], newton[:, :], var[:, :], ALU.mult).then_inc(vec_step, 1)
                vec.wait_ge(vec_step, done + 3)
                vec.scalar_tensor_tensor(out=rstd[:, :], in0=newton[:, :], scalar=1.5, in1=rstd0[:, :],
                                         op0=ALU.add, op1=ALU.mult).then_inc(vec_step, 1)

            def rows(g):
                vec.wait_ge(vec_step, (g + 1) * VEC_STEPS)
                vec.wait_ge(consts_then_rows, CONSTS + 16 * g)
                for b in range(BLOCKS):
                    vec.tensor_scalar(o_sb[:, b], z[:, b], mean[:, b:b + 1], rstd[:, b:b + 1],
                                      ALU.subtract, ALU.mult).then_inc(rows_made, 1)

            def hidden(k):
                cs = slice(k * CHUNKS, (k + 1) * CHUNKS)
                vec.wait_ge(x_loaded[k % 2], 16 * (k // 2 + 1))
                if k >= 2:
                    vec.wait_ge(h_lo_made, k - 1)
                vec.tensor_tensor(h_full[:, k % 2], x_sb[:, cs],
                                  w_sb[:, :].unsqueeze(1).to_broadcast([P, CHUNKS, F]),
                                  ALU.mult).then_inc(h_made, 1)

            vec.wait_ge(consts_then_rows, CONSTS)
            hidden(0)
            for k in range(TPG):
                if k + 1 < TPG:
                    hidden(k + 1)
                split_tile(0, k)

            def later_group(g):
                for k in range(TPG):
                    split_tile(g, k)
                    if k == STATS_AFTER:
                        residual(g - 1)
                    if k == STATS_AFTER + 1:
                        variance(g - 1)
                    if k == NORM_AFTER:
                        factor(g - 1)
                    if k == NORM_AFTER + 1:
                        rows(g - 1)

            with vec.Fori(1, GROUPS - 1) as g:
                later_group(g)
            later_group(GROUPS - 1)
            residual(GROUPS - 1)
            variance(GROUPS - 1)
            factor(GROUPS - 1)
            rows(GROUPS - 1)

        @block.tensor
        def _(pe):
            def products(g, k, bank):
                slot = k % RING
                for chunks, made in steps(g, k):
                    pe.wait_ge(hi_made, made)
                    for c in range(chunks.start, chunks.stop):
                        pe.matmul(sums[:, bank], h_hi[:, k * CHUNKS + c], a_hi[:, slot, c],
                                  start=(k == 0 and c == 0), stop=False)
                        pe.matmul(sums[:, bank], h_lo[:, k * CHUNKS + c], a_hi[:, slot, c],
                                  start=False, stop=False)
                    pe.wait_ge(lo_made, made)
                    for c in range(chunks.start, chunks.stop):
                        mm = pe.matmul(sums[:, bank], h_hi[:, k * CHUNKS + c], a_lo[:, slot, c],
                                       start=False, stop=(k == TPG - 1 and c == CHUNKS - 1))
                mm.then_inc(tile_used, 1)

            def turn(g):
                pe.wait_ge(sums_copied, g + 1)
                for b in range(BLOCKS):
                    t = pe.transpose(turned[:, b], yT[:, b * P:(b + 1) * P], ident_sb[:, :])
                t.then_inc(sums_turned, 1)

            for k in range(TPG):
                pe.wait_ge(h_lo_made, k + 1)
                products(0, k, 0)
            pe.wait_ge(consts_then_rows, CONSTS)

            def later_group(g):
                for k in range(TPG):
                    products(g, k, g % 2)
                    if k == TURN_AFTER:
                        turn(g - 1)

            with pe.Fori(1, GROUPS - 1) as g:
                later_group(g)
            later_group(GROUPS - 1)
            turn(GROUPS - 1)


def kernel(x, adj, L0_gnn_W):
    import numpy as np
    import concourse.bacc as bacc
    from concourse.bass_utils import run_bass_kernel_spmd

    n, f = x.shape
    groups, chunks = n // ROWS, n // P
    arrays = {
        "x_l": np.ascontiguousarray(np.asarray(x).reshape(chunks, P, f).transpose(1, 0, 2)),
        "adj_l": np.ascontiguousarray(
            np.asarray(adj).reshape(groups, ROWS, chunks // CHUNKS, CHUNKS, P).transpose(0, 2, 4, 3, 1)
        ).reshape(groups * chunks // CHUNKS, P, CHUNKS, ROWS),
        "w_l": np.asarray(L0_gnn_W).reshape(1, f),
        "ident_l": np.eye(P, dtype=np.float32),
    }
    nc = bacc.Bacc("TRN2", target_bir_lowering=False, num_devices=1)
    aps = [nc.dram_tensor(name, a.shape, F32, kind="ExternalInput").ap() for name, a in arrays.items()]
    out = nc.dram_tensor("out_l", [groups, P, ROWS // P, f], F32, kind="ExternalOutput").ap()
    resnorm_program(nc, *aps, out)
    r = run_bass_kernel_spmd(nc, [arrays], core_ids=[0])
    return r.results[0]["out_l"].transpose(0, 2, 1, 3).reshape(n, f)
```
